# Optimizing a Trainium2 kernel written in Bass

```python
import numpy as np
import jax
import jax.numpy as jnp

def _softmax(x, axis=-1):
    return jax.nn.softmax(x, axis=axis)
def _gelu(x):
    return jax.nn.gelu(x, approximate=True)
def _silu(x):
    return jax.nn.silu(x)
def _sigmoid(x):
    return jax.nn.sigmoid(x)
def _layernorm(x, axis=-1, eps=1e-5):
    m = jnp.mean(x, axis=axis, keepdims=True)
    v = jnp.var(x, axis=axis, keepdims=True)
    return (x - m) / jnp.sqrt(v + eps)
def _scatter_add(tgt, idx, src, axis=0):
    return tgt.at[idx].add(src)
def _segment_sum(src, seg, n):
    return jax.ops.segment_sum(src, seg, n)

kernel_name = 'mk_conv_seq_d1_conv_nchw128_a1e073'

def setup_inputs(seed: int = 0):
    np.random.seed(seed)
    _w = jnp.asarray
    def _rec_inputs():
        import jax
        import jax.numpy as jnp
        _gk = jax.random.key(seed)
        x = -0.000125 + 0.9999 * jax.random.normal(jax.random.fold_in(_gk, 1), (4, 128, 128, 512), jnp.float32)
        return x
    x = _rec_inputs()
    def _L0_conv_setup():
        import jax, jax.numpy as jnp
        import numpy as np
        EPS = 1e-06
        KH, KW = (3, 3)

        def _rmsnorm2d(x, g):
            ms = jnp.mean(jnp.square(x), axis=1, keepdims=True)
            return x * jax.lax.rsqrt(ms + EPS) * g[None, :, None, None]
        key = jax.random.key(seed)
        ks = jax.random.split(key, 5)
        B, C, F, T = (4, 128, 128, 512)
        H = 2 * C
        x = jax.random.normal(ks[0], (B, C, F, T), dtype=jnp.float32)
        g_norm = jnp.ones((C,), dtype=jnp.float32)
        w_in = jax.random.normal(ks[1], (2 * H, C), dtype=jnp.float32) * 0.05
        b_in = jnp.zeros((2 * H,), dtype=jnp.float32)
        w_dw = jax.random.normal(ks[2], (H, 1, KH, KW), dtype=jnp.float32) * 0.1
        b_dw = jnp.zeros((H,), dtype=jnp.float32)
        w_out = jax.random.normal(ks[3], (C, H), dtype=jnp.float32) * 0.05
        b_out = jnp.zeros((C,), dtype=jnp.float32)
        return {'x': x, 'g_norm': g_norm, 'w_in': w_in, 'b_in': b_in, 'w_dw': w_dw, 'b_dw': b_dw, 'w_out': w_out, 'b_out': b_out}
    _L0_conv_all = _L0_conv_setup()
    _L0_conv_in = {k: v for k, v in _L0_conv_all.items() if k in ('g_norm', 'w_in', 'b_in', 'w_dw', 'b_dw', 'w_out', 'b_out', )}
    del _L0_conv_all

    return {
        "x": x,
        "L0_conv_g_norm": _L0_conv_in["g_norm"],
        "L0_conv_w_in": _L0_conv_in["w_in"],
        "L0_conv_b_in": _L0_conv_in["b_in"],
        "L0_conv_w_dw": _L0_conv_in["w_dw"],
        "L0_conv_b_dw": _L0_conv_in["b_dw"],
        "L0_conv_w_out": _L0_conv_in["w_out"],
        "L0_conv_b_out": _L0_conv_in["b_out"],
    }

def reference(x, L0_conv_g_norm, L0_conv_w_in, L0_conv_b_in, L0_conv_w_dw, L0_conv_b_dw, L0_conv_w_out, L0_conv_b_out):
    import jax
    import jax.numpy as jnp
    def _L0_conv_ref(x, g_norm, w_in, b_in, w_dw, b_dw, w_out, b_out):
        import jax, jax.numpy as jnp
        import numpy as np
        EPS = 1e-06
        KH, KW = (3, 3)

        def _rmsnorm2d(x, g):
            ms = jnp.mean(jnp.square(x), axis=1, keepdims=True)
            return x * jax.lax.rsqrt(ms + EPS) * g[None, :, None, None]
        B, C, F, T = x.shape
        H = w_dw.shape[0]
        y = _rmsnorm2d(x, g_norm)
        ab = jnp.einsum('oc,bcft->boft', w_in, y) + b_in[None, :, None, None]
        a, b = (ab[:, :H], ab[:, H:])
        y = a * jax.nn.sigmoid(b)
        y = jax.lax.conv_general_dilated(y, w_dw, window_strides=(1, 1), padding=[((KH - 1) // 2, KH // 2), (KW - 1, 0)], dimension_numbers=('NCHW', 'OIHW', 'NCHW'), feature_group_count=H) + b_dw[None, :, None, None]
        y = jax.nn.silu(y)
        out = jnp.einsum('co,boft->bcft', w_out, y) + b_out[None, :, None, None]
        return x + out

    def _gn(v, G=32, eps=1e-5):
        B_, C_, H_, W_ = v.shape
        g = v.reshape(B_, G, C_ // G, H_, W_)
        m = jnp.mean(g, axis=(2, 3, 4), keepdims=True)
        s = jnp.var(g, axis=(2, 3, 4), keepdims=True)
        return ((g - m) / jnp.sqrt(s + eps)).reshape(v.shape)

    def _ln_c(v, eps=1e-6):
        m = jnp.mean(v, axis=1, keepdims=True)
        s = jnp.var(v, axis=1, keepdims=True)
        return (v - m) / jnp.sqrt(s + eps)

    def _ln_t(v, eps=1e-5):
        m = jnp.mean(v, axis=-1, keepdims=True)
        s = jnp.var(v, axis=-1, keepdims=True)
        return (v - m) / jnp.sqrt(s + eps)

    def _to_tokens(v):
        B_, C_, H_, W_ = v.shape
        return v.reshape(B_, C_, H_ * W_).transpose(0, 2, 1)
    def _from_tokens(t, like):
        B_, C_, H_, W_ = like.shape
        return t.transpose(0, 2, 1).reshape(B_, C_, H_, W_)

    x = _L0_conv_ref(x, L0_conv_g_norm, L0_conv_w_in, L0_conv_b_in, L0_conv_w_dw, L0_conv_b_dw, L0_conv_w_out, L0_conv_b_out)
    return x


_drawn_inputs = setup_inputs


def setup_inputs(seed=0):
    import zlib

    import numpy as np

    out = dict(_drawn_inputs(seed))
    spreads = {'L0_conv_g_norm': (1.0, 0.6),
     'L0_conv_b_in': (0.0, 0.8),
     'L0_conv_b_dw': (0.0, 0.1),
     'L0_conv_b_out': (0.0, 0.1)}
    factors = {}
    for name, (base, spread) in spreads.items():
        noise = np.random.default_rng([zlib.crc32(name.encode()), seed]).standard_normal(out[name].shape)
        drawn = base * np.exp(spread * noise) if base else spread * noise
        out[name] = jnp.asarray(drawn.astype(out[name].dtype))
    for name, factor in factors.items():
        out[name] = (out[name] * factor).astype(out[name].dtype)
    return out
```

```python
import concourse.bass as bass
from concourse import mybir
from contextlib import ExitStack

EPS = 1e-6
KH, KW = 3, 3
ROWS = 2
STEPS = 8
YRING = 4
MID_TAPS = [(1, kw) for kw in range(KW)]
SIDE_TAPS = [(2, kw) for kw in range(KW)] + [(0, kw) for kw in range(KW)]


class Step:

    def __init__(self, image, group, k, pairs, images):
        self.image, self.group, self.k, self.pairs, self.images = image, group, k, pairs, images
        self.static = isinstance(image, int) and isinstance(group, int)

    def pair(self, lag):
        return Pair(self, self.k - lag)


class Pair:

    def __init__(self, step, off):
        self.step, self.off = step, off
        self.slot = off % STEPS
        if step.static:
            at = step.image * step.pairs + step.group * STEPS + off
            self.exists = 0 <= at < step.images * step.pairs
        else:
            self.exists = True

    def count(self, per_pair, more):
        s = self.step
        return (s.image * s.pairs + s.group * STEPS) * per_pair + (self.off * per_pair + more)

    def follows(self, n):
        s = self.step
        if s.static:
            return s.image * s.pairs + s.group * STEPS + self.off >= n
        assert STEPS + self.off >= n
        return True

    def laps(self, more):
        s = self.step
        return (s.image * (s.pairs // STEPS) + s.group) * 16 + (self.off // STEPS + more) * 16

    def first_of_image(self):
        return isinstance(self.step.group, int) and (self.step.group * STEPS + self.off) % self.step.pairs == 0

    def last_of_image(self):
        return isinstance(self.step.group, int) and (self.step.group * STEPS + self.off + 1) % self.step.pairs == 0

    def place(self):
        s = self.step
        at = s.group * STEPS + self.off
        if isinstance(s.group, int) and s.group * STEPS + self.off < 0:
            return s.image - 1, at + s.pairs
        if s.static and at >= s.pairs:
            return s.image + at // s.pairs, at % s.pairs
        return s.image, at


def run_steps(engine, images, pairs, body):
    groups = pairs // STEPS

    def group(image, g):
        for k in range(STEPS):
            body(Step(image, g, k, pairs, images))

    group(0, 0)
    with engine.Fori(1, groups) as g:
        group(0, g)
    with engine.Fori(1, images) as image:
        group(image, 0)
        with engine.Fori(1, groups) as g:
            group(image, g)
    group(images, 0)


def conv_block(nc, x, g_norm, w_in_t, b_in, w_dw, b_dw, w_out_t, b_out, out):
    fp32, f32r = mybir.dt.float32, mybir.dt.float32r
    ALU, ACT = mybir.AluOpType, mybir.ActivationFunctionType
    B, C, F, T = x.shape
    HB = w_dw.shape[1]
    PAIRS = F // ROWS
    BLK = T // 128
    TP = T + KW + 1
    PAD = KW - 1
    x_v = x.rearrange("b c f t -> b c (f t)")
    out_v = out.rearrange("b c f t -> b c (f t)")
    PT = ROWS * T

    ctx = ExitStack()
    with ctx:
        def sb(name, shape, dt=fp32):
            return ctx.enter_context(nc.sbuf_tensor(name, shape, dt))

        def ps(name, shape):
            return ctx.enter_context(nc.psum_tensor(name, shape, fp32))

        def sem(name):
            return ctx.enter_context(nc.semaphore(name))

        ident = sb("ident", [128, 128])
        ident_r = sb("ident_r", [128, 128], f32r)
        ones = sb("ones", [128, 2])
        neg_half = sb("neg_half", [128, ROWS * BLK])
        unit = sb("unit", [128, ROWS * BLK])
        g_sb = sb("g_sb", [128, 1])
        win = sb("win", [128, 2 * HB * 128])
        win_hi = sb("win_hi", [128, 2 * HB * 128], f32r)
        win_lo = sb("win_lo", [128, 2 * HB * 128], f32r)
        wout = sb("wout", [128, HB, 128])
        wout_hi = sb("wout_hi", [128, HB, 128], f32r)
        wout_lo = sb("wout_lo", [128, HB, 128], f32r)
        wdw = sb("wdw", [128, HB, KH * KW])
        diag = sb("diag", [128, 128])
        diag_hi = sb("diag_hi", [128, HB, len(MID_TAPS), 128], f32r)
        diag_lo = sb("diag_lo", [128, HB, len(MID_TAPS), 128], f32r)
        bin_sb = sb("bin_sb", [128, 2 * HB])
        bin_half = sb("bin_half", [128, 2 * HB])
        bdw_sb = sb("bdw_sb", [128, HB])
        bout_sb = sb("bout_sb", [128, 1])

        xr = sb("xr", [128, STEPS, PT])
        xsq = sb("xsq", [128, 2, PT])
        ms_sb = sb("ms_sb", [128, 2, ROWS * BLK])
        rinv = sb("rinv", [128, ROWS * BLK])
        rinv_hi = sb("rinv_hi", [128, 2, ROWS * BLK], f32r)
        rinv_lo = sb("rinv_lo", [128, 2, ROWS * BLK], f32r)
        xn = sb("xn", [128, 2, T])
        xn_hi = sb("xn_hi", [128, 2, T], f32r)
        xn_lo = sb("xn_lo", [128, 2, T], f32r)
        th = sb("th", [128, 2, HB, T])
        ah = sb("ah", [128, 2, HB, T])
        y = sb("y", [128, HB, YRING * ROWS, TP])
        y_hi = sb("y_hi", [128, HB, 2 * ROWS, TP], f32r)
        y_lo = sb("y_lo", [128, HB, 2 * ROWS, TP], f32r)
        z = sb("z", [128, HB, PT])
        z_hi = sb("z_hi", [128, HB, 2, PT], f32r)
        z_lo = sb("z_lo", [128, HB, 2, PT], f32r)
        o = sb("o", [128, 2, T])

        p_norm = ps("p_norm", [128, T])
        p_b = ps("p_b", [128, T])
        p_a = ps("p_a", [128, T])
        p_o = ps("p_o", [128, T])
        p_conv = [ps(f"p_conv{h}", [128, ROWS, T]) for h in range(HB)]

        weights_loaded = sem("weights_loaded")
        ident_zero, ident_ready = sem("ident_zero"), sem("ident_ready")
        setup = sem("setup")
        weights_ready = sem("weights_ready")
        x_loaded = [sem(f"x_loaded{i}") for i in range(STEPS)]
        stored = [sem(f"stored{i}") for i in range(STEPS)]
        sq_ready, ms_ready, ms_read = sem("sq_ready"), sem("ms_ready"), sem("ms_read")
        pow_ready, rhi_ready, rinv_ready = sem("pow_ready"), sem("rhi_ready"), sem("rinv_ready")
        bc_ready = sem("bc_ready")
        xn_ready, xn_hi_ready, xn_lo_ready = sem("xn_ready"), sem("xn_hi_ready"), sem("xn_lo_ready")
        b_ready, a_ready, th_ready, ah_ready = sem("b_ready"), sem("a_ready"), sem("th_ready"), sem("ah_ready")
        y_ready, y_hi_ready, y_lo_ready = sem("y_ready"), sem("y_hi_ready"), sem("y_lo_ready")
        conv_ready = sem("conv_ready")
        tap_done = sem("tap_done")
        z_ready, z_hi_ready, z_lo_ready = sem("z_ready"), sem("z_hi_ready"), sem("z_lo_ready")
        p_o_ready, o_ready, out_ready = sem("p_o_ready"), sem("o_ready"), sem("out_ready")
        NT = len(SIDE_TAPS)
        LOADS = 7

        block = ctx.enter_context(nc.Block())

        @block.sync
        def _(sp):
            for dst, src in ((win[:, :], w_in_t), (g_sb[:, :], g_norm), (bin_sb[:, :], b_in),
                             (wdw[:, :, :], w_dw), (bdw_sb[:, :], b_dw), (wout[:, :, :], w_out_t),
                             (bout_sb[:, :], b_out)):
                sp.dma_start(dst, src).then_inc(weights_loaded, 16)

            def body(s):
                q, p = s.pair(STEPS), s.pair(0)
                if q.exists:
                    image, at = q.place()
                    sp.wait_ge(out_ready, q.count(2, 2))
                    sp.dma_start(out_v[bass.ds(image, 1), :, bass.ds(at * PT, PT)].rearrange("o c n -> c (o n)"),
                                 xr[:, q.slot, :]).then_inc(stored[q.slot], 16)
                if p.exists:
                    image, at = p.place()
                    if p.follows(STEPS):
                        sp.wait_ge(stored[p.slot], p.laps(0))
                    sp.dma_start(xr[:, p.slot, :],
                                 x_v[bass.ds(image, 1), :, bass.ds(at * PT, PT)].rearrange("o c n -> c (o n)")
                                 ).then_inc(x_loaded[p.slot], 16)

            run_steps(sp, B, PAIRS, body)
            for i in range(STEPS):
                sp.wait_ge(stored[i], 16 * B * PAIRS // STEPS)

        @block.gpsimd
        def _(pool):
            nc.gpsimd.memset(ident[:, :], 0.0).then_inc(ident_zero, 1)
            pool.wait_ge(ident_zero, 1)
            nc.gpsimd.affine_select(out=ident[:, :], in_=ident[:, :], compare_op=ALU.not_equal, fill=1.0,
                                    base=0, pattern=[[-1, 128]], channel_multiplier=1).then_inc(ident_ready, 1)
            nc.gpsimd.memset(neg_half[:, :], -0.5).then_inc(ident_ready, 1)
            nc.gpsimd.memset(unit[:, :], 1.0).then_inc(ident_ready, 1)
            pool.wait_ge(ident_ready, 3)

            def rinv_parts(p):
                if not p.exists:
                    return
                pool.wait_ge(ms_read, p.count(1, 1))
                if p.follows(2):
                    pool.wait_ge(bc_ready, p.count(2, -2))
                nc.gpsimd.tensor_tensor(rinv[:, :], ms_sb[:, p.slot % 2, :], neg_half[:, :], ALU.pow
                                        ).then_inc(pow_ready, 1)
                pool.wait_ge(pow_ready, p.count(1, 1))
                nc.gpsimd.tensor_tensor(rinv_hi[:, p.slot % 2, :], rinv[:, :], unit[:, :], ALU.mult
                                        ).then_inc(rhi_ready, 1)
                pool.wait_ge(rhi_ready, p.count(1, 1))
                nc.gpsimd.tensor_tensor(rinv_lo[:, p.slot % 2, :], rinv[:, :],
                                        rinv_hi[:, p.slot % 2, :].bitcast(fp32), ALU.subtract
                                        ).then_inc(rinv_ready, 1)

            def y_low(p, r):
                if not p.exists:
                    return
                pool.wait_ge(y_hi_ready, p.count(2, r + 1))
                a, b = (p.slot % YRING) * ROWS + r, (p.slot % 2) * ROWS + r
                nc.gpsimd.tensor_tensor(y_lo[:, :, b, PAD:PAD + T], y[:, :, a, PAD:PAD + T],
                                        y_hi[:, :, b, PAD:PAD + T].bitcast(fp32), ALU.subtract
                                        ).then_inc(y_lo_ready, 1)

            def xn_low(p, r):
                if not p.exists:
                    return
                pool.wait_ge(xn_hi_ready, p.count(2, r + 1))
                nc.gpsimd.tensor_tensor(xn_lo[:, r, :], xn[:, r, :], xn_hi[:, r, :].bitcast(fp32),
                                        ALU.subtract).then_inc(xn_lo_ready, 1)

            def z_low(p, h):
                if not p.exists:
                    return
                pool.wait_ge(z_hi_ready, p.count(2, h + 1))
                nc.gpsimd.tensor_tensor(z_lo[:, h, p.slot % 2, :], z[:, h, :],
                                        z_hi[:, h, p.slot % 2, :].bitcast(fp32), ALU.subtract
                                        ).then_inc(z_lo_ready, 1)

            def add_x(p, r):
                if not p.exists:
                    return
                pool.wait_ge(o_ready, p.count(2, r + 1))
                xs = xr[:, p.slot, r * T:(r + 1) * T]
                nc.gpsimd.tensor_tensor(xs, o[:, r, :], xs, ALU.add).then_inc(out_ready, 1)

            def body(s):
                y_low(s.pair(3), 1)
                add_x(s.pair(6), 0)
                z_low(s.pair(5), 1)
                rinv_parts(s.pair(0))
                xn_low(s.pair(1), 0)

                y_low(s.pair(2), 0)
                add_x(s.pair(6), 1)
                z_low(s.pair(4), 0)
                xn_low(s.pair(1), 1)

            run_steps(pool, B, PAIRS, body)

        @block.scalar
        def _(act):
            act.wait_ge(weights_ready, 1)

            def square(p):
                if not p.exists:
                    return
                act.wait_ge(x_loaded[p.slot], p.laps(1))
                if p.follows(2):
                    act.wait_ge(ms_ready, p.count(1, -1))
                nc.scalar.activation(xsq[:, p.slot % 2, :], xr[:, p.slot, :], ACT.Square).then_inc(sq_ready, 1)

            def xn_high(p, r):
                if not p.exists:
                    return
                act.wait_ge(xn_ready, p.count(2, r + 1))
                if p.follows(1):
                    act.wait_ge(a_ready, p.count(4, 2 * r - 2))
                nc.scalar.activation(xn_hi[:, r, :], xn[:, r, :], ACT.Copy).then_inc(xn_hi_ready, 1)

            def gate_inputs(p, r, h):
                if not p.exists:
                    return
                if p.follows(1):
                    act.wait_ge(y_ready, p.count(2, r - 1))
                act.wait_ge(b_ready, p.count(4, 2 * r + h + 1))
                nc.scalar.activation(th[:, r, h, :], p_b[:, :], ACT.Tanh, bias=bin_half[:, HB + h:HB + h + 1],
                                     scale=0.5).then_inc(th_ready, 1)
                act.wait_ge(a_ready, p.count(4, 2 * r + h + 1))
                nc.scalar.activation(ah[:, r, h, :], p_a[:, :], ACT.Identity, bias=bin_half[:, h:h + 1],
                                     scale=0.5).then_inc(ah_ready, 1)

            def y_high(p, r):
                if not p.exists:
                    return
                act.wait_ge(y_ready, p.count(2, r + 1))
                if p.follows(2):
                    act.wait_ge(conv_ready, p.count(2, -2))
                a, b = (p.slot % YRING) * ROWS + r, (p.slot % 2) * ROWS + r
                nc.scalar.activation(y_hi[:, :, b, PAD:PAD + T], y[:, :, a, PAD:PAD + T], ACT.Copy
                                     ).then_inc(y_hi_ready, 1)

            def silu(p, h):
                if not p.exists:
                    return
                act.wait_ge(tap_done, p.count(2 * NT, (h + 1) * NT))
                if p.follows(1):
                    act.wait_ge(z_lo_ready, p.count(2, h - 1))
                nc.scalar.activation(z[:, h, :], p_conv[h][:, :, :].rearrange("p r t -> p (r t)"), ACT.Silu,
                                     bias=bdw_sb[:, h:h + 1]).then_inc(z_ready, 1)

            def z_high(p, h):
                if not p.exists:
                    return
                act.wait_ge(z_ready, p.count(2, h + 1))
                if p.follows(2):
                    act.wait_ge(p_o_ready, p.count(2, -2))
                nc.scalar.activation(z_hi[:, h, p.slot % 2, :], z[:, h, :], ACT.Copy).then_inc(z_hi_ready, 1)

            def projected(p, r):
                if not p.exists:
                    return
                act.wait_ge(p_o_ready, p.count(2, r + 1))
                if p.follows(1):
                    act.wait_ge(out_ready, p.count(2, r - 1))
                nc.scalar.activation(o[:, r, :], p_o[:, :], ACT.Identity, bias=bout_sb[:, 0:1]
                                     ).then_inc(o_ready, 1)

            def body(s):
                y_high(s.pair(3), 1)
                gate_inputs(s.pair(2), 0, 0)
                silu(s.pair(5), 1)
                square(s.pair(0))
                gate_inputs(s.pair(2), 0, 1)
                z_high(s.pair(5), 1)
                xn_high(s.pair(1), 0)
                projected(s.pair(6), 1)

                y_high(s.pair(2), 0)
                gate_inputs(s.pair(2), 1, 0)
                silu(s.pair(4), 0)
                gate_inputs(s.pair(2), 1, 1)
                z_high(s.pair(4), 0)
                xn_high(s.pair(1), 1)
                projected(s.pair(5), 0)

            run_steps(act, B, PAIRS, body)

        @block.vector
        def _(dve):
            n = [0]

            def link(ins):
                n[0] += 1
                ins.then_inc(setup, 1)
                dve.wait_ge(setup, n[0])

            def split(hi, lo, src):
                link(nc.vector.tensor_copy(hi, src))
                link(nc.vector.tensor_tensor(lo, src, hi.bitcast(fp32), ALU.subtract))

            nc.vector.memset(ones[:, :], 1.0)
            nc.vector.memset(y[:, :, :, 0:PAD], 0.0)
            nc.vector.memset(y_hi[:, :, :, 0:PAD].bitcast(fp32), 0.0)
            link(nc.vector.memset(y_lo[:, :, :, 0:PAD].bitcast(fp32), 0.0))
            dve.wait_ge(weights_loaded, 16 * LOADS)
            dve.wait_ge(ident_ready, 3)
            link(nc.vector.tensor_copy(ident_r[:, :], ident[:, :]))
            link(nc.vector.tensor_scalar(bin_half[:, :], bin_sb[:, :], 0.5, None, ALU.mult))
            link(nc.vector.tensor_scalar(win[:, :], win[:, :], g_sb[:, 0:1], None, ALU.mult))
            split(win_hi[:, :], win_lo[:, :], win[:, :])
            split(wout_hi[:, :, :], wout_lo[:, :, :], wout[:, :, :])
            for h in range(HB):
                for i, (kh, kw) in enumerate(MID_TAPS):
                    tap = kh * KW + kw
                    link(nc.vector.tensor_scalar(diag[:, :], ident[:, :], wdw[:, h, tap:tap + 1], None, ALU.mult))
                    split(diag_hi[:, h, i, :], diag_lo[:, h, i, :], diag[:, :])
            nc.vector.memset(diag[:, 0:1], 0.0).then_inc(weights_ready, 1)

            def mean_squares(p):
                if not p.exists:
                    return
                dve.wait_ge(ms_ready, p.count(1, 1))
                if p.follows(2):
                    dve.wait_ge(rinv_ready, p.count(1, -1))
                nc.vector.tensor_scalar(ms_sb[:, p.slot % 2, :], p_norm[:, 0:ROWS * BLK], 1.0 / C, EPS,
                                        ALU.mult, ALU.add).then_inc(ms_read, 1)

            def normalise(p, r):
                if not p.exists:
                    return
                dve.wait_ge(bc_ready, p.count(2, r + 1))
                if p.follows(1):
                    dve.wait_ge(xn_lo_ready, p.count(2, r - 1))
                nc.vector.tensor_tensor(xn[:, r, :], xr[:, p.slot, r * T:(r + 1) * T], p_norm[:, :],
                                        ALU.mult).then_inc(xn_ready, 1)

            def gate(p, r):
                if not p.exists:
                    return
                dve.wait_ge(th_ready, p.count(4, 2 * r + 2))
                dve.wait_ge(ah_ready, p.count(4, 2 * r + 2))
                if p.follows(4):
                    dve.wait_ge(y_lo_ready, p.count(2, r - 7))
                nc.vector.scalar_tensor_tensor(out=y[:, :, (p.slot % YRING) * ROWS + r, PAD:PAD + T],
                                               in0=th[:, r, :, :], scalar=1.0, in1=ah[:, r, :, :],
                                               op0=ALU.add, op1=ALU.mult).then_inc(y_ready, 1)

            def taps(p, h, which):
                if not p.exists:
                    return
                for i in which:
                    kh, kw = SIDE_TAPS[i]
                    if i == 0:
                        dve.wait_ge(conv_ready, p.count(2, h + 1))
                        if not (p.step.static and not p.step.pair(p.step.k - p.off - 1).exists):
                            dve.wait_ge(y_ready, p.count(2, 4))
                    else:
                        dve.wait_ge(tap_done, p.count(2 * NT, h * NT + i))
                    rows = [r for r in range(ROWS)
                            if not (kh == 0 and r == 0 and p.first_of_image())
                            and not (kh == 2 and r == ROWS - 1 and p.last_of_image())]
                    at = [((p.slot % YRING) * ROWS + r + kh - 1) % (YRING * ROWS) for r in rows]
                    runs = [(rows[0], at[0], len(rows))]
                    if len(rows) == 2 and at[1] != at[0] + 1:
                        runs = [(rows[0], at[0], 1), (rows[1], at[1], 1)]
                    tap = kh * KW + kw
                    for r, a, k in runs:
                        acc = p_conv[h][:, r:r + k, :]
                        last = nc.vector.scalar_tensor_tensor(
                            out=acc, in0=y[:, h, a:a + k, kw:kw + T], scalar=wdw[:, h, tap:tap + 1],
                            in1=acc, op0=ALU.mult, op1=ALU.add)
                    last.then_inc(tap_done, 1)

            def body(s):
                normalise(s.pair(1), 0)
                taps(s.pair(4), 0, range(0, NT // 2))
                gate(s.pair(2), 0)
                mean_squares(s.pair(0))
                taps(s.pair(4), 0, range(NT // 2, NT))

                normalise(s.pair(1), 1)
                taps(s.pair(4), 1, range(0, NT // 2))
                gate(s.pair(2), 1)
                taps(s.pair(4), 1, range(NT // 2, NT))

            run_steps(dve, B, PAIRS, body)

        @block.tensor
        def _(pe):
            pe.wait_ge(weights_ready, 1)

            def three_pass(psum, parts):
                todo = [m for w_hi, w_lo, v_hi, v_lo in parts for m in ((w_lo, v_hi), (w_hi, v_hi), (w_hi, v_lo))]
                for i, (w, v) in enumerate(todo):
                    last = nc.tensor.matmul(psum, w, v, start=(i == 0), stop=(i == len(todo) - 1))
                return last

            def sum_squares(p):
                if not p.exists:
                    return
                pe.wait_ge(sq_ready, p.count(1, 1))
                if p.follows(1):
                    pe.wait_ge(xn_ready, p.count(2, -1))
                for j in range(ROWS * BLK):
                    last = nc.tensor.matmul(p_norm[:, j:j + 1], xsq[:, p.slot % 2, j * 128:(j + 1) * 128],
                                            ones[:, 0:1], start=True, stop=True)
                last.then_inc(ms_ready, 1)

            def broadcast(p, r):
                if not p.exists:
                    return
                pe.wait_ge(rinv_ready, p.count(1, 1))
                if p.follows(1) or r:
                    pe.wait_ge(xn_ready, p.count(2, r))
                if r == 1 and not (p.step.static and not p.step.pair(p.step.k - p.off - 1).exists):
                    pe.wait_ge(ms_read, p.count(1, 2))
                for j in range(BLK):
                    col = r * BLK + j
                    psum = p_norm[:, j * 128:(j + 1) * 128]
                    nc.tensor.matmul(psum, rinv_hi[:, p.slot % 2, col:col + 1].to_broadcast([128, 128]),
                                     ident_r[:, :], start=True, stop=False)
                    last = nc.tensor.matmul(psum, rinv_lo[:, p.slot % 2, col:col + 1].to_broadcast([128, 128]),
                                            ident_r[:, :], start=False, stop=True)
                last.then_inc(bc_ready, 1)

            def project_in(p, r, h):
                if not p.exists:
                    return
                pe.wait_ge(xn_hi_ready, p.count(2, r + 1))
                pe.wait_ge(xn_lo_ready, p.count(2, r + 1))
                if p.follows(1) or r or h:
                    pe.wait_ge(th_ready, p.count(4, 2 * r + h))
                cols = slice((HB + h) * 128, (HB + h + 1) * 128)
                three_pass(p_b[:, :], [(win_hi[:, cols], win_lo[:, cols], xn_hi[:, r, :], xn_lo[:, r, :])]
                           ).then_inc(b_ready, 1)
                if p.follows(1) or r or h:
                    pe.wait_ge(ah_ready, p.count(4, 2 * r + h))
                cols = slice(h * 128, (h + 1) * 128)
                three_pass(p_a[:, :], [(win_hi[:, cols], win_lo[:, cols], xn_hi[:, r, :], xn_lo[:, r, :])]
                           ).then_inc(a_ready, 1)

            def conv(p, h):
                if not p.exists:
                    return
                pe.wait_ge(y_hi_ready, p.count(2, 2))
                pe.wait_ge(y_lo_ready, p.count(2, 2))
                if p.follows(1):
                    pe.wait_ge(z_ready, p.count(2, h - 1))
                for r in range(ROWS):
                    b = (p.slot % 2) * ROWS + r
                    last = three_pass(p_conv[h][:, r, :],
                                      [(diag_hi[:, h, i, :], diag_lo[:, h, i, :],
                                        y_hi[:, h, b, kw:kw + T], y_lo[:, h, b, kw:kw + T])
                                       for i, (kh, kw) in enumerate(MID_TAPS)])
                last.then_inc(conv_ready, 1)

            def project_out(p, r):
                if not p.exists:
                    return
                pe.wait_ge(z_hi_ready, p.count(2, 2))
                pe.wait_ge(z_lo_ready, p.count(2, 2))
                if p.follows(1) or r:
                    pe.wait_ge(o_ready, p.count(2, r))
                cols = slice(r * T, (r + 1) * T)
                three_pass(p_o[:, :], [(wout_hi[:, h, :], wout_lo[:, h, :], z_hi[:, h, p.slot % 2, cols],
                                        z_lo[:, h, p.slot % 2, cols]) for h in range(HB)]
                           ).then_inc(p_o_ready, 1)

            def body(s):
                broadcast(s.pair(1), 0)
                project_in(s.pair(2), 0, 0)
                project_out(s.pair(6), 1)
                project_in(s.pair(2), 0, 1)
                sum_squares(s.pair(0))
                conv(s.pair(4), 1)

                broadcast(s.pair(1), 1)
                project_in(s.pair(2), 1, 0)
                project_out(s.pair(5), 0)
                project_in(s.pair(2), 1, 1)
                conv(s.pair(3), 0)

            run_steps(pe, B, PAIRS, body)


def kernel(x, L0_conv_g_norm, L0_conv_w_in, L0_conv_b_in, L0_conv_w_dw, L0_conv_b_dw, L0_conv_w_out, L0_conv_b_out):
    import numpy as np
    import concourse.bacc as bacc
    from concourse.bass_utils import run_bass_kernel_spmd

    x = np.ascontiguousarray(x)
    C = x.shape[1]
    H = L0_conv_w_dw.shape[0]
    HB = H // 128
    arrays = {
        "x": x,
        "g_norm": np.ascontiguousarray(L0_conv_g_norm).reshape(C, 1),
        "w_in_t": np.ascontiguousarray(np.asarray(L0_conv_w_in).T),
        "b_in": np.ascontiguousarray(np.asarray(L0_conv_b_in).reshape(2 * HB, 128).T),
        "w_dw": np.ascontiguousarray(np.asarray(L0_conv_w_dw).reshape(HB, 128, KH * KW).transpose(1, 0, 2)),
        "b_dw": np.ascontiguousarray(np.asarray(L0_conv_b_dw).reshape(HB, 128).T),
        "w_out_t": np.ascontiguousarray(np.asarray(L0_conv_w_out).T.reshape(HB, 128, C).transpose(1, 0, 2)),
        "b_out": np.ascontiguousarray(L0_conv_b_out).reshape(C, 1),
    }
    nc = bacc.Bacc("TRN2", target_bir_lowering=False, num_devices=1)
    args = [nc.dram_tensor(name, a.shape, mybir.dt.from_np(a.dtype), kind="ExternalInput").ap()
            for name, a in arrays.items()]
    out = nc.dram_tensor("out", x.shape, mybir.dt.float32, kind="ExternalOutput").ap()
    conv_block(nc, *args, out)
    r = run_bass_kernel_spmd(nc, [arrays], core_ids=[0])
    return r.results[0]["out"]
```

```python
import concourse.bass as bass
from concourse import mybir
from contextlib import ExitStack

EPS = 1e-6
KH, KW = 3, 3
ROWS = 2
STEPS = 8
YRING = 4
SPLIT_H = 0
MID_TAPS = [(1, kw) for kw in range(KW)]
SIDE_TAPS = [(2, kw) for kw in range(KW)] + [(0, kw) for kw in range(KW)]


class Step:

    def __init__(self, image, group, k, pairs, images):
        self.image, self.group, self.k, self.pairs, self.images = image, group, k, pairs, images
        self.static = isinstance(image, int) and isinstance(group, int)

    def pair(self, lag):
        return Pair(self, self.k - lag)


class Pair:

    def __init__(self, step, off):
        self.step, self.off = step, off
        self.slot = off % STEPS
        if step.static:
            at = step.image * step.pairs + step.group * STEPS + off
            self.exists = 0 <= at < step.images * step.pairs
        else:
            self.exists = True

    def count(self, per_pair, more):
        s = self.step
        return (s.image * s.pairs + s.group * STEPS) * per_pair + (self.off * per_pair + more)

    def follows(self, n):
        s = self.step
        if s.static:
            return s.image * s.pairs + s.group * STEPS + self.off >= n
        assert STEPS + self.off >= n
        return True

    def laps(self, more):
        s = self.step
        return (s.image * (s.pairs // STEPS) + s.group) * 16 + (self.off // STEPS + more) * 16

    def laps2(self, more):
        s = self.step
        return (s.image * s.pairs + s.group * STEPS) * 8 + (self.off // 2 + more) * 16

    def first_of_image(self):
        return isinstance(self.step.group, int) and (self.step.group * STEPS + self.off) % self.step.pairs == 0

    def last_of_image(self):
        return isinstance(self.step.group, int) and (self.step.group * STEPS + self.off + 1) % self.step.pairs == 0

    def place(self):
        s = self.step
        at = s.group * STEPS + self.off
        if isinstance(s.group, int) and s.group * STEPS + self.off < 0:
            return s.image - 1, at + s.pairs
        if s.static and at >= s.pairs:
            return s.image + at // s.pairs, at % s.pairs
        return s.image, at


def run_steps(engine, images, pairs, body):
    groups = pairs // STEPS

    def group(image, g):
        for k in range(STEPS):
            body(Step(image, g, k, pairs, images))

    group(0, 0)
    with engine.Fori(1, groups) as g:
        group(0, g)
    with engine.Fori(1, images) as image:
        group(image, 0)
        with engine.Fori(1, groups) as g:
            group(image, g)
    group(images, 0)


def conv_block(nc, x, g_norm, w_in_t, b_in, w_dw, b_dw, w_out_t, b_out, out):
    fp32, f32r = mybir.dt.float32, mybir.dt.float32r
    ALU, ACT = mybir.AluOpType, mybir.ActivationFunctionType
    B, C, F, T = x.shape
    HB = w_dw.shape[1]
    PAIRS = F // ROWS
    PT = ROWS * T
    TPP = PT // 128
    GV = T // 4
    TP = T + KW + 1
    PAD = KW - 1
    x_v = x.rearrange("b c f t -> b c (f t)")
    out_v = out.rearrange("b c f t -> b c (f t)")
    rinv_dram = nc.dram_tensor("rinv_dram", [2, PT], fp32).ap()

    ctx = ExitStack()
    with ctx:
        def sb(name, shape, dt=fp32):
            return ctx.enter_context(nc.sbuf_tensor(name, shape, dt))

        def ps(name, shape):
            return ctx.enter_context(nc.psum_tensor(name, shape, fp32))

        def sem(name):
            return ctx.enter_context(nc.semaphore(name))

        ident = sb("ident", [128, 128])
        ones = sb("ones", [128, 2])
        neg_half = sb("neg_half", [128, TPP])
        g_sb = sb("g_sb", [128, 1])
        win = sb("win", [128, 2 * HB * 128])
        win_hi = sb("win_hi", [128, 2 * HB * 128], f32r)
        win_lo = sb("win_lo", [128, 2 * HB * 128], f32r)
        wout = sb("wout", [128, HB, 128])
        wout_hi = sb("wout_hi", [128, 128], f32r)
        wout_lo = sb("wout_lo", [128, 128], f32r)
        wdw = sb("wdw", [128, HB, KH * KW])
        diag = sb("diag", [128, 128])
        diag_hi = sb("diag_hi", [128, HB, len(MID_TAPS), 128], f32r)
        diag_lo = sb("diag_lo", [128, HB, len(MID_TAPS), 128], f32r)
        bin_sb = sb("bin_sb", [128, 2 * HB])
        bin_half = sb("bin_half", [128, 2 * HB])
        half = sb("half", [128, 1])
        bdw_sb = sb("bdw_sb", [128, HB])
        bout_sb = sb("bout_sb", [128, 1])

        xr = sb("xr", [128, STEPS, PT])
        xsq = sb("xsq", [128, 2, PT])
        ms_sb = sb("ms_sb", [128, 2, TPP])
        rinv = sb("rinv", [128, 2, TPP])
        rinv_b = sb("rinv_b", [128, 2, PT])
        xn = sb("xn", [128, 2, T])
        xn_hi = sb("xn_hi", [128, 2, T], f32r)
        xn_lo = sb("xn_lo", [128, 2, T], f32r)
        sig = sb("sig", [128, 2, HB, T])
        ab = sb("ab", [128, 2, HB, T])
        y = sb("y", [128, HB, YRING * ROWS, TP])
        y_hi = sb("y_hi", [128, HB, 2 * ROWS, TP], f32r)
        y_lo = sb("y_lo", [128, HB, 2 * ROWS, TP], f32r)
        z = sb("z", [128, HB, 2, PT])
        z_hi = sb("z_hi", [128, 2, PT], f32r)
        z_lo = sb("z_lo", [128, 2, PT], f32r)
        o = sb("o", [128, 2, T])

        p_norm = ps("p_norm", [128, T])
        p_b = ps("p_b", [128, T])
        p_a = ps("p_a", [128, T])
        p_o = ps("p_o", [128, T])
        p_conv = [ps(f"p_conv{h}", [128, ROWS, T]) for h in range(HB)]

        weights_loaded = sem("weights_loaded")
        ident_zero, ident_ready = sem("ident_zero"), sem("ident_ready")
        setup = sem("setup")
        weights_ready = sem("weights_ready")
        x_loaded = [sem(f"x_loaded{i}") for i in range(STEPS)]
        stored = [sem(f"stored{i}") for i in range(STEPS)]
        sq_ready, ms_ready, ms_read = sem("sq_ready"), sem("ms_ready"), sem("ms_read")
        rinv_ready = sem("rinv_ready")
        rinv_out = [sem(f"rinv_out{i}") for i in range(2)]
        rinv_in = [sem(f"rinv_in{i}") for i in range(2)]
        xn_ready, xn_hi_ready, xn_lo_ready = sem("xn_ready"), sem("xn_hi_ready"), sem("xn_lo_ready")
        b_ready, a_ready = sem("b_ready"), sem("a_ready")
        tanh_ready, sig_ready, ab_ready = sem("tanh_ready"), sem("sig_ready"), sem("ab_ready")
        y_ready, y_side_ready = sem("y_ready"), sem("y_side_ready")
        y_hi_ready, y_lo_ready = sem("y_hi_ready"), sem("y_lo_ready")
        conv_ready = sem("conv_ready")
        tap_done = sem("tap_done")
        z_ready, z_hi_ready, z_lo_ready = sem("z_ready"), sem("z_hi_ready"), sem("z_lo_ready")
        p_o_ready, o_ready, out_ready = sem("p_o_ready"), sem("o_ready"), sem("out_ready")
        NT = len(SIDE_TAPS)
        LOADS = 7

        block = ctx.enter_context(nc.Block())

        @block.sync
        def _(sp):
            for dst, src in ((win[:, :], w_in_t), (g_sb[:, :], g_norm), (bin_sb[:, :], b_in),
                             (wdw[:, :, :], w_dw), (bdw_sb[:, :], b_dw), (wout[:, :, :], w_out_t),
                             (bout_sb[:, :], b_out)):
                sp.dma_start(dst, src).then_inc(weights_loaded, 16)

            def body(s):
                q, p = s.pair(STEPS), s.pair(0)
                if q.exists:
                    image, at = q.place()
                    sp.wait_ge(out_ready, q.count(2, 2))
                    sp.dma_start(out_v[bass.ds(image, 1), :, bass.ds(at * PT, PT)].rearrange("o c n -> c (o n)"),
                                 xr[:, q.slot, :]).then_inc(stored[q.slot], 16)
                if p.exists:
                    image, at = p.place()
                    if p.follows(STEPS):
                        sp.wait_ge(stored[p.slot], p.laps(0))
                    sp.dma_start(xr[:, p.slot, :],
                                 x_v[bass.ds(image, 1), :, bass.ds(at * PT, PT)].rearrange("o c n -> c (o n)")
                                 ).then_inc(x_loaded[p.slot], 16)
                p = s.pair(1)
                if p.exists:
                    i = p.slot % 2
                    sp.wait_ge(rinv_ready, p.count(1, 1))
                    sp.dma_start(rinv_dram[i, :].rearrange("(p j) -> p j", j=TPP), rinv[:, i, :]
                                 ).then_inc(rinv_out[i], 16)
                    sp.wait_ge(rinv_out[i], p.laps2(1))
                    sp.dma_start(rinv_b[:, i, :], rinv_dram[i:i + 1, :].to_broadcast([128, PT])
                                 ).then_inc(rinv_in[i], 16)

            run_steps(sp, B, PAIRS, body)
            for i in range(STEPS):
                sp.wait_ge(stored[i], 16 * B * PAIRS // STEPS)

        @block.gpsimd
        def _(pool):
            nc.gpsimd.memset(ident[:, :], 0.0).then_inc(ident_zero, 1)
            pool.wait_ge(ident_zero, 1)
            nc.gpsimd.affine_select(out=ident[:, :], in_=ident[:, :], compare_op=ALU.not_equal, fill=1.0,
                                    base=0, pattern=[[-1, 128]], channel_multiplier=1).then_inc(ident_ready, 1)
            nc.gpsimd.memset(neg_half[:, :], -0.5).then_inc(ident_ready, 1)
            pool.wait_ge(ident_ready, 2)

            def inverse_rms(p):
                if not p.exists:
                    return
                pool.wait_ge(ms_read, p.count(1, 1))
                if p.follows(2):
                    pool.wait_ge(xn_ready, p.count(2, -2))
                nc.gpsimd.tensor_tensor(rinv[:, p.slot % 2, :], ms_sb[:, p.slot % 2, :], neg_half[:, :],
                                        ALU.pow).then_inc(rinv_ready, 1)

            def y_low(p, r):
                if not p.exists:
                    return
                pool.wait_ge(y_hi_ready, p.count(2, r + 1))
                a, b = (p.slot % YRING) * ROWS + r, (p.slot % 2) * ROWS + r
                nc.gpsimd.tensor_tensor(y_lo[:, :, b, PAD:PAD + T], y[:, :, a, PAD:PAD + T],
                                        y_hi[:, :, b, PAD:PAD + T].bitcast(fp32), ALU.subtract
                                        ).then_inc(y_lo_ready, 1)

            def xn_low(p, r):
                if not p.exists:
                    return
                pool.wait_ge(xn_hi_ready, p.count(2, r + 1))
                nc.gpsimd.tensor_tensor(xn_lo[:, r, :], xn[:, r, :], xn_hi[:, r, :].bitcast(fp32),
                                        ALU.subtract).then_inc(xn_lo_ready, 1)

            def gate(p, r):
                if not p.exists:
                    return
                pool.wait_ge(sig_ready, p.count(2, r + 1))
                pool.wait_ge(ab_ready, p.count(4, 2 * r + 2))
                if p.follows(YRING):
                    pool.wait_ge(tap_done, p.count(2 * NT, -(YRING - 2) * 2 * NT))
                nc.gpsimd.tensor_tensor(y[:, :, (p.slot % YRING) * ROWS + r, PAD:PAD + T - GV],
                                        sig[:, r, :, 0:T - GV], ab[:, r, :, 0:T - GV], ALU.mult
                                        ).then_inc(y_ready, 1)

            def z_low(p):
                if not p.exists:
                    return
                pool.wait_ge(z_hi_ready, p.count(1, 1))
                nc.gpsimd.tensor_tensor(z_lo[:, p.slot % 2, :], z[:, SPLIT_H, p.slot % 2, :],
                                        z_hi[:, p.slot % 2, :].bitcast(fp32), ALU.subtract
                                        ).then_inc(z_lo_ready, 1)

            def add_x(p, r):
                if not p.exists:
                    return
                pool.wait_ge(o_ready, p.count(2, r + 1))
                xs = xr[:, p.slot, r * T:(r + 1) * T]
                nc.gpsimd.tensor_tensor(xs, o[:, r, :], xs, ALU.add).then_inc(out_ready, 1)

            def body(s):
                xn_low(s.pair(2), 1)
                add_x(s.pair(6), 0)
                y_low(s.pair(3), 1)
                z_low(s.pair(5))
                gate(s.pair(2), 0)

                xn_low(s.pair(1), 0)
                add_x(s.pair(6), 1)
                inverse_rms(s.pair(0))
                y_low(s.pair(2), 0)
                gate(s.pair(2), 1)

            run_steps(pool, B, PAIRS, body)

        @block.scalar
        def _(act):
            act.wait_ge(weights_ready, 1)

            def square(p):
                if not p.exists:
                    return
                act.wait_ge(x_loaded[p.slot], p.laps(1))
                if p.follows(2):
                    act.wait_ge(ms_ready, p.count(1, -1))
                nc.scalar.activation(xsq[:, p.slot % 2, :], xr[:, p.slot, :], ACT.Square).then_inc(sq_ready, 1)

            def xn_high(p, r):
                if not p.exists:
                    return
                act.wait_ge(xn_ready, p.count(2, r + 1))
                if p.follows(1):
                    act.wait_ge(a_ready, p.count(4, 2 * r - 2))
                nc.scalar.activation(xn_hi[:, r, :], xn[:, r, :], ACT.Copy).then_inc(xn_hi_ready, 1)

            def gate_inputs(p, r, h):
                if not p.exists:
                    return
                if p.follows(1):
                    act.wait_ge(y_ready, p.count(2, r - 1))
                    act.wait_ge(y_side_ready, p.count(2, r - 1))
                act.wait_ge(b_ready, p.count(4, 2 * r + h + 1))
                nc.scalar.activation(sig[:, r, h, :], p_b[:, :], ACT.Tanh, bias=bin_half[:, HB + h:HB + h + 1],
                                     scale=0.5).then_inc(tanh_ready, 1)
                act.wait_ge(a_ready, p.count(4, 2 * r + h + 1))
                nc.scalar.activation(ab[:, r, h, :], p_a[:, :], ACT.Identity, bias=bin_sb[:, h:h + 1]
                                     ).then_inc(ab_ready, 1)

            def sigmoid(p, r):
                if not p.exists:
                    return
                act.wait_ge(tanh_ready, p.count(4, 2 * r + 2))
                nc.scalar.activation(sig[:, r, :, :], sig[:, r, :, :], ACT.Identity, bias=half[:, 0:1],
                                     scale=0.5).then_inc(sig_ready, 1)

            def y_high(p, r):
                if not p.exists:
                    return
                act.wait_ge(y_ready, p.count(2, r + 1))
                act.wait_ge(y_side_ready, p.count(2, r + 1))
                if p.follows(2):
                    act.wait_ge(conv_ready, p.count(2, -2))
                a, b = (p.slot % YRING) * ROWS + r, (p.slot % 2) * ROWS + r
                nc.scalar.activation(y_hi[:, :, b, PAD:PAD + T], y[:, :, a, PAD:PAD + T], ACT.Copy
                                     ).then_inc(y_hi_ready, 1)

            def silu(p, h):
                if not p.exists:
                    return
                act.wait_ge(tap_done, p.count(2 * NT, (h + 1) * NT))
                if p.follows(2):
                    act.wait_ge(p_o_ready, p.count(2, -2))
                nc.scalar.activation(z[:, h, p.slot % 2, :], p_conv[h][:, :, :].rearrange("p r t -> p (r t)"),
                                     ACT.Silu, bias=bdw_sb[:, h:h + 1]).then_inc(z_ready, 1)

            def z_high(p):
                if not p.exists:
                    return
                act.wait_ge(z_ready, p.count(2, SPLIT_H + 1))
                nc.scalar.activation(z_hi[:, p.slot % 2, :], z[:, SPLIT_H, p.slot % 2, :], ACT.Copy
                                     ).then_inc(z_hi_ready, 1)

            def projected(p, r):
                if not p.exists:
                    return
                act.wait_ge(p_o_ready, p.count(2, r + 1))
                if p.follows(1):
                    act.wait_ge(out_ready, p.count(2, r - 1))
                nc.scalar.activation(o[:, r, :], p_o[:, :], ACT.Identity, bias=bout_sb[:, 0:1]
                                     ).then_inc(o_ready, 1)

            def body(s):
                gate_inputs(s.pair(2), 0, 0)
                silu(s.pair(5), 1)
                y_high(s.pair(3), 1)
                square(s.pair(0))
                gate_inputs(s.pair(2), 0, 1)
                sigmoid(s.pair(2), 0)
                xn_high(s.pair(1), 0)
                projected(s.pair(6), 1)

                gate_inputs(s.pair(2), 1, 0)
                silu(s.pair(4), 0)
                y_high(s.pair(2), 0)
                gate_inputs(s.pair(2), 1, 1)
                sigmoid(s.pair(2), 1)
                z_high(s.pair(4))
                xn_high(s.pair(1), 1)
                projected(s.pair(5), 0)

            run_steps(act, B, PAIRS, body)

        @block.vector
        def _(dve):
            n = [0]

            def link(ins):
                n[0] += 1
                ins.then_inc(setup, 1)
                dve.wait_ge(setup, n[0])

            def split(hi, lo, src):
                link(nc.vector.tensor_copy(hi, src))
                link(nc.vector.tensor_tensor(lo, src, hi.bitcast(fp32), ALU.subtract))

            nc.vector.memset(ones[:, :], 1.0)
            nc.vector.memset(y[:, :, :, 0:PAD], 0.0)
            nc.vector.memset(y_hi[:, :, :, 0:PAD].bitcast(fp32), 0.0)
            link(nc.vector.memset(y_lo[:, :, :, 0:PAD].bitcast(fp32), 0.0))
            dve.wait_ge(weights_loaded, 16 * LOADS)
            dve.wait_ge(ident_ready, 2)
            link(nc.vector.tensor_scalar(bin_half[:, :], bin_sb[:, :], 0.5, None, ALU.mult))
            link(nc.vector.tensor_scalar(win[:, :], win[:, :], g_sb[:, 0:1], None, ALU.mult))
            split(win_hi[:, :], win_lo[:, :], win[:, :])
            split(wout_hi[:, :], wout_lo[:, :], wout[:, SPLIT_H, :])
            nc.vector.memset(half[:, :], 0.5)
            for h in range(HB):
                for i, (kh, kw) in enumerate(MID_TAPS):
                    tap = kh * KW + kw
                    link(nc.vector.tensor_scalar(diag[:, :], ident[:, :], wdw[:, h, tap:tap + 1], None, ALU.mult))
                    split(diag_hi[:, h, i, :], diag_lo[:, h, i, :], diag[:, :])
            nc.vector.memset(diag[:, 0:1], 0.0).then_inc(weights_ready, 1)

            def mean_squares(p):
                if not p.exists:
                    return
                dve.wait_ge(ms_ready, p.count(1, 1))
                if p.follows(2):
                    dve.wait_ge(rinv_ready, p.count(1, -1))
                nc.vector.tensor_scalar(ms_sb[:, p.slot % 2, :], p_norm[:, 0:TPP], 1.0 / C, EPS,
                                        ALU.mult, ALU.add).then_inc(ms_read, 1)

            def normalise(p, r):
                if not p.exists:
                    return
                dve.wait_ge(rinv_in[p.slot % 2], p.laps2(1))
                if p.follows(1):
                    dve.wait_ge(xn_lo_ready, p.count(2, r - 1))
                nc.vector.tensor_tensor(xn[:, r, :], xr[:, p.slot, r * T:(r + 1) * T],
                                        rinv_b[:, p.slot % 2, r * T:(r + 1) * T],
                                        ALU.mult).then_inc(xn_ready, 1)

            def gate_side(p, r):
                if not p.exists:
                    return
                dve.wait_ge(sig_ready, p.count(2, r + 1))
                dve.wait_ge(ab_ready, p.count(4, 2 * r + 2))
                if p.follows(YRING):
                    dve.wait_ge(y_lo_ready, p.count(2, r + 1 - 2 * YRING))
                nc.vector.tensor_tensor(y[:, :, (p.slot % YRING) * ROWS + r, PAD + T - GV:PAD + T],
                                        sig[:, r, :, T - GV:T], ab[:, r, :, T - GV:T], ALU.mult
                                        ).then_inc(y_side_ready, 1)

            def taps(p, h, which):
                if not p.exists:
                    return
                for i in which:
                    kh, kw = SIDE_TAPS[i]
                    if i == 0:
                        dve.wait_ge(conv_ready, p.count(2, h + 1))
                        if not (p.step.static and not p.step.pair(p.step.k - p.off - 1).exists):
                            dve.wait_ge(y_ready, p.count(2, 4))
                            dve.wait_ge(y_side_ready, p.count(2, 4))
                    else:
                        dve.wait_ge(tap_done, p.count(2 * NT, h * NT + i))
                    rows = [r for r in range(ROWS)
                            if not (kh == 0 and r == 0 and p.first_of_image())
                            and not (kh == 2 and r == ROWS - 1 and p.last_of_image())]
                    at = [((p.slot % YRING) * ROWS + r + kh - 1) % (YRING * ROWS) for r in rows]
                    runs = [(rows[0], at[0], len(rows))]
                    if len(rows) == 2 and at[1] != at[0] + 1:
                        runs = [(rows[0], at[0], 1), (rows[1], at[1], 1)]
                    tap = kh * KW + kw
                    for r, a, k in runs:
                        acc = p_conv[h][:, r:r + k, :]
                        last = nc.vector.scalar_tensor_tensor(
                            out=acc, in0=y[:, h, a:a + k, kw:kw + T], scalar=wdw[:, h, tap:tap + 1],
                            in1=acc, op0=ALU.mult, op1=ALU.add)
                    last.then_inc(tap_done, 1)

            def body(s):
                taps(s.pair(4), 0, range(0, 2))
                normalise(s.pair(1), 0)
                taps(s.pair(4), 0, range(2, 5))
                gate_side(s.pair(2), 0)
                taps(s.pair(4), 0, range(5, NT))

                mean_squares(s.pair(0))
                taps(s.pair(4), 1, range(0, 2))
                normalise(s.pair(1), 1)
                taps(s.pair(4), 1, range(2, 5))
                gate_side(s.pair(2), 1)
                taps(s.pair(4), 1, range(5, NT))

            run_steps(dve, B, PAIRS, body)

        @block.tensor
        def _(pe):
            pe.wait_ge(weights_ready, 1)

            def three_pass(psum, parts, first=True, last=True):
                todo = [m for w_hi, w_lo, v_hi, v_lo in parts for m in ((w_lo, v_hi), (w_hi, v_hi), (w_hi, v_lo))]
                for i, (w, v) in enumerate(todo):
                    ins = nc.tensor.matmul(psum, w, v, start=first and i == 0, stop=last and i == len(todo) - 1)
                return ins

            def sum_squares(p):
                if not p.exists:
                    return
                pe.wait_ge(sq_ready, p.count(1, 1))
                if p.follows(1):
                    pe.wait_ge(ms_read, p.count(1, 0))
                tokens = xsq[:, p.slot % 2, :].rearrange("c (p j) -> c j p", j=TPP)
                for j in range(TPP):
                    last = nc.tensor.matmul(p_norm[:, j:j + 1], tokens[:, j, :], ones[:, 0:1],
                                            start=True, stop=True)
                last.then_inc(ms_ready, 1)

            def project_in(p, r, h):
                if not p.exists:
                    return
                pe.wait_ge(xn_hi_ready, p.count(2, r + 1))
                pe.wait_ge(xn_lo_ready, p.count(2, r + 1))
                if p.follows(1) or r or h:
                    pe.wait_ge(tanh_ready, p.count(4, 2 * r + h))
                cols = slice((HB + h) * 128, (HB + h + 1) * 128)
                three_pass(p_b[:, :], [(win_hi[:, cols], win_lo[:, cols], xn_hi[:, r, :], xn_lo[:, r, :])]
                           ).then_inc(b_ready, 1)
                if p.follows(1) or r or h:
                    pe.wait_ge(ab_ready, p.count(4, 2 * r + h))
                cols = slice(h * 128, (h + 1) * 128)
                three_pass(p_a[:, :], [(win_hi[:, cols], win_lo[:, cols], xn_hi[:, r, :], xn_lo[:, r, :])]
                           ).then_inc(a_ready, 1)

            def conv(p, h):
                if not p.exists:
                    return
                pe.wait_ge(y_hi_ready, p.count(2, 2))
                pe.wait_ge(y_lo_ready, p.count(2, 2))
                if p.follows(1):
                    pe.wait_ge(z_ready, p.count(2, h - 1))
                for r in range(ROWS):
                    b = (p.slot % 2) * ROWS + r
                    last = three_pass(p_conv[h][:, r, :],
                                      [(diag_hi[:, h, i, :], diag_lo[:, h, i, :],
                                        y_hi[:, h, b, kw:kw + T], y_lo[:, h, b, kw:kw + T])
                                       for i, (kh, kw) in enumerate(MID_TAPS)])
                last.then_inc(conv_ready, 1)

            def project_out(p, r):
                if not p.exists:
                    return
                pe.wait_ge(z_ready, p.count(2, 2))
                if p.follows(1) or r:
                    pe.wait_ge(o_ready, p.count(2, r))
                cols = slice(r * T, (r + 1) * T)
                pe.wait_ge(z_lo_ready, p.count(1, 1))
                for h in range(HB):
                    if h == SPLIT_H:
                        last = three_pass(p_o[:, :], [(wout_hi[:, :], wout_lo[:, :], z_hi[:, p.slot % 2, cols],
                                                       z_lo[:, p.slot % 2, cols])], h == 0, h == HB - 1)
                    else:
                        last = nc.tensor.matmul(p_o[:, :], wout[:, h, :], z[:, h, p.slot % 2, cols],
                                                start=(h == 0), stop=(h == HB - 1))
                last.then_inc(p_o_ready, 1)

            def body(s):
                project_in(s.pair(2), 0, 0)
                project_out(s.pair(6), 1)
                project_in(s.pair(2), 0, 1)
                conv(s.pair(4), 1)
                sum_squares(s.pair(0))

                project_in(s.pair(2), 1, 0)
                project_out(s.pair(5), 0)
                project_in(s.pair(2), 1, 1)
                conv(s.pair(3), 0)

            run_steps(pe, B, PAIRS, body)


def kernel(x, L0_conv_g_norm, L0_conv_w_in, L0_conv_b_in, L0_conv_w_dw, L0_conv_b_dw, L0_conv_w_out, L0_conv_b_out):
    import numpy as np
    import concourse.bacc as bacc
    from concourse.bass_utils import run_bass_kernel_spmd

    x = np.ascontiguousarray(x)
    C = x.shape[1]
    H = L0_conv_w_dw.shape[0]
    HB = H // 128
    arrays = {
        "x": x,
        "g_norm": np.ascontiguousarray(L0_conv_g_norm).reshape(C, 1),
        "w_in_t": np.ascontiguousarray(np.asarray(L0_conv_w_in).T),
        "b_in": np.ascontiguousarray(np.asarray(L0_conv_b_in).reshape(2 * HB, 128).T),
        "w_dw": np.ascontiguousarray(np.asarray(L0_conv_w_dw).reshape(HB, 128, KH * KW).transpose(1, 0, 2)),
        "b_dw": np.ascontiguousarray(np.asarray(L0_conv_b_dw).reshape(HB, 128).T),
        "w_out_t": np.ascontiguousarray(np.asarray(L0_conv_w_out).T.reshape(HB, 128, C).transpose(1, 0, 2)),
        "b_out": np.ascontiguousarray(L0_conv_b_out).reshape(C, 1),
    }
    nc = bacc.Bacc("TRN2", target_bir_lowering=False, num_devices=1)
    args = [nc.dram_tensor(name, a.shape, mybir.dt.from_np(a.dtype), kind="ExternalInput").ap()
            for name, a in arrays.items()]
    out = nc.dram_tensor("out", x.shape, mybir.dt.float32, kind="ExternalOutput").ap()
    conv_block(nc, *args, out)
    r = run_bass_kernel_spmd(nc, [arrays], core_ids=[0])
    return r.results[0]["out"]
```

```python
import concourse.bass as bass
from concourse import mybir
from contextlib import ExitStack

EPS = 1e-6
KH, KW = 3, 3
ROWS = 2
STEPS = 8
YRING = 4
MID = [(1, kw) for kw in range(KW)]
SIDE = [(kh, kw) for kh in (0, 2) for kw in range(KW)]
OWN, SHARED = (2, 0), (0, 1)
FIRST = MID[0]
PE_TAPS = [tap for tap in SIDE if tap != OWN]
TAPS = [MID + [OWN, SHARED], MID[1:] + SIDE]


class Step:

    def __init__(self, image, group, k, pairs, images):
        self.image, self.group, self.k, self.pairs, self.images = image, group, k, pairs, images
        self.static = isinstance(image, int) and isinstance(group, int)

    def pair(self, lag):
        return Pair(self, self.k - lag)


class Pair:

    def __init__(self, step, off):
        self.step, self.off = step, off
        self.slot = off % STEPS
        if step.static:
            at = step.image * step.pairs + step.group * STEPS + off
            self.exists = 0 <= at < step.images * step.pairs
        else:
            self.exists = True

    def count(self, per_pair, more):
        s = self.step
        return (s.image * s.pairs + s.group * STEPS) * per_pair + (self.off * per_pair + more)

    def follows(self, n):
        s = self.step
        if s.static:
            return s.image * s.pairs + s.group * STEPS + self.off >= n
        assert STEPS + self.off >= n
        return True

    def laps(self, more):
        s = self.step
        return (s.image * (s.pairs // STEPS) + s.group) * 16 + (self.off // STEPS + more) * 16

    def laps2(self, more):
        s = self.step
        return (s.image * s.pairs + s.group * STEPS) * 8 + (self.off // 2 + more) * 16

    def first_of_image(self):
        return isinstance(self.step.group, int) and (self.step.group * STEPS + self.off) % self.step.pairs == 0

    def last_of_image(self):
        return isinstance(self.step.group, int) and (self.step.group * STEPS + self.off + 1) % self.step.pairs == 0

    def next_exists(self):
        return Pair(self.step, self.off + 1).exists

    def tap_rows(self, kh):
        return [r for r in range(ROWS)
                if not (kh == 0 and r == 0 and self.first_of_image())
                and not (kh == 2 and r == ROWS - 1 and self.last_of_image())]

    def place(self):
        s = self.step
        at = s.group * STEPS + self.off
        if isinstance(s.group, int) and s.group * STEPS + self.off < 0:
            return s.image - 1, at + s.pairs
        if s.static and at >= s.pairs:
            return s.image + at // s.pairs, at % s.pairs
        return s.image, at


def run_steps(engine, images, pairs, body):
    groups = pairs // STEPS

    def group(image, g):
        for k in range(STEPS):
            body(Step(image, g, k, pairs, images))

    group(0, 0)
    with engine.Fori(1, groups) as g:
        group(0, g)
    with engine.Fori(1, images) as image:
        group(image, 0)
        with engine.Fori(1, groups) as g:
            group(image, g)
    group(images, 0)


def conv_block(nc, x, g_norm, w_in_t, b_in, w_dw, b_dw, w_out_t, b_out, out):
    fp32, f32r = mybir.dt.float32, mybir.dt.float32r
    ALU, ACT = mybir.AluOpType, mybir.ActivationFunctionType
    B, C, F, T = x.shape
    HB = w_dw.shape[1]
    PAIRS = F // ROWS
    PT = ROWS * T
    TPP = PT // 128
    SHARED_COLS = [T // 2, 0]
    TP = T + KW + 1
    PAD = KW - 1
    x_v = x.rearrange("b c f t -> b c (f t)")
    out_v = out.rearrange("b c f t -> b c (f t)")
    rinv_dram = nc.dram_tensor("rinv_dram", [2, PT], fp32).ap()

    ctx = ExitStack()
    with ctx:
        def sb(name, shape, dt=fp32):
            return ctx.enter_context(nc.sbuf_tensor(name, shape, dt))

        def ps(name, shape):
            return ctx.enter_context(nc.psum_tensor(name, shape, fp32))

        def sem(name):
            return ctx.enter_context(nc.semaphore(name))

        ident = sb("ident", [128, 128])
        ones = sb("ones", [128, 2])
        neg_half = sb("neg_half", [128, TPP])
        g_sb = sb("g_sb", [128, 1])
        win = sb("win", [128, 2 * HB * 128])
        win_hi = sb("win_hi", [128, 2 * HB * 128], f32r)
        win_lo = sb("win_lo", [128, 2 * HB * 128], f32r)
        wout = sb("wout", [128, HB, 128])
        wdw = sb("wdw", [128, HB, KH * KW])
        diag = sb("diag", [128, 128])
        diag_hi = sb("diag_hi", [128, len(PE_TAPS), 128], f32r)
        diag_lo = sb("diag_lo", [128, len(PE_TAPS), 128], f32r)
        bin_sb = sb("bin_sb", [128, 2 * HB])
        bin_half = sb("bin_half", [128, 2 * HB])
        half = sb("half", [128, 1])
        bdw_sb = sb("bdw_sb", [128, HB])
        bout_sb = sb("bout_sb", [128, 1])

        xr = sb("xr", [128, STEPS, PT])
        xsq = sb("xsq", [128, 2, PT])
        ms_sb = sb("ms_sb", [128, 2, TPP])
        rinv = sb("rinv", [128, 2, TPP])
        rinv_b = sb("rinv_b", [128, 2, PT])
        xn = sb("xn", [128, PT])
        xn_hi = sb("xn_hi", [128, 2, PT], f32r)
        xn_lo = sb("xn_lo", [128, 2, PT], f32r)
        sig = sb("sig", [128, 2, HB, T])
        ab = sb("ab", [128, 2, HB, T])
        y = sb("y", [128, HB, YRING * ROWS, TP])
        y_hi = sb("y_hi", [128, YRING * ROWS, TP], f32r)
        y_lo = sb("y_lo", [128, YRING * ROWS, TP], f32r)
        u = sb("u", [128, 2, ROWS, T])
        z = sb("z", [128, HB, 2, PT])
        o = sb("o", [128, 2, T])

        p_norm = ps("p_norm", [128, T])
        p_b = ps("p_b", [128, T])
        p_a = ps("p_a", [128, T])
        p_o = ps("p_o", [128, T])
        p_conv = [ps(f"p_conv{i}", [128, ROWS, T]) for i in range(2)]

        weights_loaded = sem("weights_loaded")
        ident_zero, ident_ready = sem("ident_zero"), sem("ident_ready")
        setup = sem("setup")
        weights_ready = sem("weights_ready")
        x_loaded = [sem(f"x_loaded{i}") for i in range(STEPS)]
        stored = [sem(f"stored{i}") for i in range(STEPS)]
        sq_ready, ms_ready, ms_read = sem("sq_ready"), sem("ms_ready"), sem("ms_read")
        rinv_ready = sem("rinv_ready")
        rinv_out = [sem(f"rinv_out{i}") for i in range(2)]
        rinv_in = [sem(f"rinv_in{i}") for i in range(2)]
        xn_ready, xn_hi_ready, xn_lo_ready = sem("xn_ready"), sem("xn_hi_ready"), sem("xn_lo_ready")
        b_ready, a_ready = sem("b_ready"), sem("a_ready")
        tanh_ready, sig_ready, ab_ready = sem("tanh_ready"), sem("sig_ready"), sem("ab_ready")
        y_ready, y_hi_ready, y_lo_ready = sem("y_ready"), sem("y_hi_ready"), sem("y_lo_ready")
        conv_ready = sem("conv_ready")
        first_done = sem("first_done")
        tap_done = [sem(f"tap{h}_done") for h in range(HB)]
        z_ready = [sem(f"z{h}_ready") for h in range(HB)]
        p_o_ready, o_ready, out_ready = sem("p_o_ready"), sem("o_ready"), sem("out_ready")
        LOADS = 7

        block = ctx.enter_context(nc.Block())

        @block.sync
        def _(sp):
            for dst, src in ((win[:, :], w_in_t), (g_sb[:, :], g_norm), (bin_sb[:, :], b_in),
                             (wdw[:, :, :], w_dw), (bdw_sb[:, :], b_dw), (wout[:, :, :], w_out_t),
                             (bout_sb[:, :], b_out)):
                sp.dma_start(dst, src).then_inc(weights_loaded, 16)

            def body(s):
                q, p = s.pair(STEPS), s.pair(0)
                if q.exists:
                    image, at = q.place()
                    sp.wait_ge(out_ready, q.count(1, 1))
                    sp.dma_start(out_v[bass.ds(image, 1), :, bass.ds(at * PT, PT)].rearrange("o c n -> c (o n)"),
                                 xr[:, q.slot, :]).then_inc(stored[q.slot], 16)
                if p.exists:
                    image, at = p.place()
                    if p.follows(STEPS):
                        sp.wait_ge(stored[p.slot], p.laps(0))
                    sp.dma_start(xr[:, p.slot, :],
                                 x_v[bass.ds(image, 1), :, bass.ds(at * PT, PT)].rearrange("o c n -> c (o n)")
                                 ).then_inc(x_loaded[p.slot], 16)
                p = s.pair(1)
                if p.exists:
                    i = p.slot % 2
                    sp.wait_ge(rinv_ready, p.count(1, 1))
                    sp.dma_start(rinv_dram[i, :].rearrange("(p j) -> p j", j=TPP), rinv[:, i, :]
                                 ).then_inc(rinv_out[i], 16)
                    sp.wait_ge(rinv_out[i], p.laps2(1))
                    sp.dma_start(rinv_b[:, i, :], rinv_dram[i:i + 1, :].to_broadcast([128, PT])
                                 ).then_inc(rinv_in[i], 16)

            run_steps(sp, B, PAIRS, body)
            for i in range(STEPS):
                sp.wait_ge(stored[i], 16 * B * PAIRS // STEPS)

        @block.gpsimd
        def _(pool):
            nc.gpsimd.memset(ident[:, :], 0.0).then_inc(ident_zero, 1)
            pool.wait_ge(ident_zero, 1)
            nc.gpsimd.affine_select(out=ident[:, :], in_=ident[:, :], compare_op=ALU.not_equal, fill=1.0,
                                    base=0, pattern=[[-1, 128]], channel_multiplier=1).then_inc(ident_ready, 1)
            nc.gpsimd.memset(neg_half[:, :], -0.5).then_inc(ident_ready, 1)
            pool.wait_ge(ident_ready, 2)

            def inverse_rms(p):
                if not p.exists:
                    return
                pool.wait_ge(ms_read, p.count(1, 1))
                if p.follows(2):
                    pool.wait_ge(xn_ready, p.count(1, -1))
                nc.gpsimd.tensor_tensor(rinv[:, p.slot % 2, :], ms_sb[:, p.slot % 2, :], neg_half[:, :],
                                        ALU.pow).then_inc(rinv_ready, 1)

            def y_low(p):
                if not p.exists:
                    return
                pool.wait_ge(y_hi_ready, p.count(1, 1))
                rows = slice((p.slot % YRING) * ROWS, (p.slot % YRING + 1) * ROWS)
                nc.gpsimd.tensor_tensor(y_lo[:, rows, PAD:PAD + T], y[:, 0, rows, PAD:PAD + T],
                                        y_hi[:, rows, PAD:PAD + T].bitcast(fp32), ALU.subtract
                                        ).then_inc(y_lo_ready, 1)

            def normalise(p):
                if not p.exists:
                    return
                pool.wait_ge(rinv_in[p.slot % 2], p.laps2(1))
                if p.follows(1):
                    pool.wait_ge(xn_lo_ready, p.count(1, 0))
                nc.gpsimd.tensor_tensor(xn[:, :], xr[:, p.slot, :], rinv_b[:, p.slot % 2, :], ALU.mult
                                        ).then_inc(xn_ready, 1)

            def xn_low(p):
                if not p.exists:
                    return
                pool.wait_ge(xn_hi_ready, p.count(1, 1))
                nc.gpsimd.tensor_tensor(xn_lo[:, p.slot % 2, :], xn[:, :], xn_hi[:, p.slot % 2, :].bitcast(fp32),
                                        ALU.subtract).then_inc(xn_lo_ready, 1)

            def gate(p, r):
                if not p.exists:
                    return
                pool.wait_ge(sig_ready, p.count(2, r + 1))
                pool.wait_ge(ab_ready, p.count(4, 2 * r + 2))
                if p.follows(YRING):
                    pool.wait_ge(tap_done[0], p.count(len(TAPS[0]), (1 + r - YRING) * len(TAPS[0])))
                    pool.wait_ge(tap_done[1], p.count(len(TAPS[1]), (2 - YRING) * len(TAPS[1])))
                nc.gpsimd.tensor_tensor(y[:, :, (p.slot % YRING) * ROWS + r, PAD:PAD + T],
                                        sig[:, r, :, :], ab[:, r, :, :], ALU.mult).then_inc(y_ready, 1)

            def add_x(p):
                if not p.exists:
                    return
                pool.wait_ge(o_ready, p.count(2, 2))
                nc.gpsimd.tensor_tensor(xr[:, p.slot, :], o[:, :, :].rearrange("p r t -> p (r t)"), xr[:, p.slot, :],
                                        ALU.add).then_inc(out_ready, 1)

            def body(s):
                add_x(s.pair(7))
                normalise(s.pair(1))
                gate(s.pair(2), 0)
                y_low(s.pair(3))

                inverse_rms(s.pair(0))
                xn_low(s.pair(1))
                gate(s.pair(2), 1)

            run_steps(pool, B, PAIRS, body)

        @block.scalar
        def _(act):
            act.wait_ge(weights_ready, 1)

            def square(p):
                if not p.exists:
                    return
                act.wait_ge(x_loaded[p.slot], p.laps(1))
                if p.follows(2):
                    act.wait_ge(ms_ready, p.count(1, -1))
                nc.scalar.activation(xsq[:, p.slot % 2, :], xr[:, p.slot, :], ACT.Square).then_inc(sq_ready, 1)

            def xn_high(p):
                if not p.exists:
                    return
                act.wait_ge(xn_ready, p.count(1, 1))
                if p.follows(2):
                    act.wait_ge(a_ready, p.count(4, -4))
                nc.scalar.activation(xn_hi[:, p.slot % 2, :], xn[:, :], ACT.Copy).then_inc(xn_hi_ready, 1)

            def gate_inputs(p, r, h):
                if not p.exists:
                    return
                if p.follows(1):
                    act.wait_ge(y_ready, p.count(2, r - 1))
                act.wait_ge(b_ready, p.count(4, 2 * r + h + 1))
                nc.scalar.activation(sig[:, r, h, :], p_b[:, :], ACT.Tanh, bias=bin_half[:, HB + h:HB + h + 1],
                                     scale=0.5).then_inc(tanh_ready, 1)
                act.wait_ge(a_ready, p.count(4, 2 * r + h + 1))
                nc.scalar.activation(ab[:, r, h, :], p_a[:, :], ACT.Identity, bias=bin_sb[:, h:h + 1]
                                     ).then_inc(ab_ready, 1)

            def sigmoid(p, r):
                if not p.exists:
                    return
                act.wait_ge(tanh_ready, p.count(4, 2 * r + 2))
                nc.scalar.activation(sig[:, r, :, :], sig[:, r, :, :], ACT.Identity, bias=half[:, 0:1],
                                     scale=0.5).then_inc(sig_ready, 1)

            def y_high(p):
                if not p.exists:
                    return
                act.wait_ge(y_ready, p.count(2, 2))
                if p.follows(YRING):
                    act.wait_ge(conv_ready, p.count(2, 2 * (2 - YRING)))
                rows = slice((p.slot % YRING) * ROWS, (p.slot % YRING + 1) * ROWS)
                nc.scalar.activation(y_hi[:, rows, PAD:PAD + T], y[:, 0, rows, PAD:PAD + T], ACT.Copy
                                     ).then_inc(y_hi_ready, 1)

            def silu(p, h):
                if not p.exists:
                    return
                act.wait_ge(tap_done[h], p.count(len(TAPS[h]), len(TAPS[h])))
                if p.follows(2):
                    act.wait_ge(p_o_ready, p.count(2, -2))
                conv = (p_conv[p.slot % 2] if h == 0 else u[:, p.slot % 2])[:, :, :].rearrange("p r t -> p (r t)")
                nc.scalar.activation(z[:, h, p.slot % 2, :], conv, ACT.Silu, bias=bdw_sb[:, h:h + 1]
                                     ).then_inc(z_ready[h], 1)

            def first_tap(p):
                if not p.exists:
                    return
                act.wait_ge(y_ready, p.count(2, 2))
                if p.follows(2):
                    act.wait_ge(z_ready[1], p.count(1, -1))
                a, (kh, kw) = (p.slot % YRING) * ROWS, FIRST
                nc.scalar.activation(u[:, p.slot % 2, :, :], y[:, 1, a:a + ROWS, kw:kw + T], ACT.Copy,
                                     scale=wdw[:, 1, kh * KW + kw:kh * KW + kw + 1]).then_inc(first_done, 1)

            def projected(p, r):
                if not p.exists:
                    return
                act.wait_ge(p_o_ready, p.count(2, r + 1))
                if p.follows(1):
                    act.wait_ge(out_ready, p.count(1, 0))
                nc.scalar.activation(o[:, r, :], p_o[:, :], ACT.Identity, bias=bout_sb[:, 0:1]
                                     ).then_inc(o_ready, 1)

            def body(s):
                gate_inputs(s.pair(2), 0, 0)
                square(s.pair(0))
                gate_inputs(s.pair(2), 0, 1)
                sigmoid(s.pair(2), 0)
                silu(s.pair(5), 1)
                y_high(s.pair(3))
                projected(s.pair(6), 0)
                xn_high(s.pair(1))

                gate_inputs(s.pair(2), 1, 0)
                gate_inputs(s.pair(2), 1, 1)
                sigmoid(s.pair(2), 1)
                silu(s.pair(5), 0)
                projected(s.pair(6), 1)
                first_tap(s.pair(3))

            run_steps(act, B, PAIRS, body)

        @block.vector
        def _(dve):
            n = [0]

            def link(ins):
                n[0] += 1
                ins.then_inc(setup, 1)
                dve.wait_ge(setup, n[0])

            def split(hi, lo, src):
                link(nc.vector.tensor_copy(hi, src))
                link(nc.vector.tensor_tensor(lo, src, hi.bitcast(fp32), ALU.subtract))

            nc.vector.memset(ones[:, :], 1.0)
            nc.vector.memset(y[:, :, :, 0:PAD], 0.0)
            nc.vector.memset(y_hi[:, :, 0:PAD].bitcast(fp32), 0.0)
            link(nc.vector.memset(y_lo[:, :, 0:PAD].bitcast(fp32), 0.0))
            dve.wait_ge(weights_loaded, 16 * LOADS)
            dve.wait_ge(ident_ready, 2)
            link(nc.vector.tensor_scalar(bin_half[:, :], bin_sb[:, :], 0.5, None, ALU.mult))
            link(nc.vector.tensor_scalar(win[:, :], win[:, :], g_sb[:, 0:1], None, ALU.mult))
            split(win_hi[:, :], win_lo[:, :], win[:, :])
            nc.vector.memset(half[:, :], 0.5)
            for i, (kh, kw) in enumerate(PE_TAPS):
                tap = kh * KW + kw
                link(nc.vector.tensor_scalar(diag[:, :], ident[:, :], wdw[:, 0, tap:tap + 1], None, ALU.mult))
                split(diag_hi[:, i, :], diag_lo[:, i, :], diag[:, :])
            nc.vector.memset(diag[:, 0:1], 0.0).then_inc(weights_ready, 1)

            def mean_squares(p):
                if not p.exists:
                    return
                dve.wait_ge(ms_ready, p.count(1, 1))
                if p.follows(2):
                    dve.wait_ge(rinv_ready, p.count(1, -1))
                nc.vector.tensor_scalar(ms_sb[:, p.slot % 2, :], p_norm[:, 0:TPP], 1.0 / C, EPS,
                                        ALU.mult, ALU.add).then_inc(ms_read, 1)

            def tap(p, h, i):
                if not p.exists:
                    return
                kh, kw = TAPS[h][i]
                if i > 0:
                    dve.wait_ge(tap_done[h], p.count(len(TAPS[h]), i))
                elif h == 0:
                    dve.wait_ge(conv_ready, p.count(2, 2))
                else:
                    dve.wait_ge(first_done, p.count(1, 1))
                if h == 1 and (kh, kw) == (2, 0) and p.next_exists():
                    dve.wait_ge(y_ready, p.count(2, 3))
                rows = p.tap_rows(kh)
                at = [((p.slot % YRING) * ROWS + r + kh - 1) % (YRING * ROWS) for r in rows]
                runs = [(rows[0], at[0], len(rows))]
                shared = h == 0 and (kh, kw) == SHARED
                if len(rows) == 2 and (shared or at[1] != at[0] + 1):
                    runs = [(rows[0], at[0], 1), (rows[1], at[1], 1)]
                w = wdw[:, h, kh * KW + kw:kh * KW + kw + 1]
                for r, a, k in runs:
                    c = SHARED_COLS[r] if shared else 0
                    acc = (p_conv[p.slot % 2] if h == 0 else u[:, p.slot % 2])[:, r:r + k, c:T]
                    src = y[:, h, a:a + k, kw + c:kw + T]
                    last = nc.vector.scalar_tensor_tensor(out=acc, in0=src, scalar=w, in1=acc,
                                                          op0=ALU.mult, op1=ALU.add)
                last.then_inc(tap_done[h], 1)

            def body(s):
                tap(s.pair(5), 0, 0)
                tap(s.pair(4), 1, 0)
                tap(s.pair(5), 0, 1)
                tap(s.pair(4), 1, 1)
                tap(s.pair(5), 0, 2)
                tap(s.pair(4), 1, 2)
                mean_squares(s.pair(0))
                tap(s.pair(4), 1, 3)

                tap(s.pair(5), 0, 3)
                tap(s.pair(4), 1, 4)
                tap(s.pair(5), 0, 4)
                tap(s.pair(4), 1, 5)
                tap(s.pair(4), 1, 6)
                tap(s.pair(4), 1, 7)

            run_steps(dve, B, PAIRS, body)

        @block.tensor
        def _(pe):
            pe.wait_ge(weights_ready, 1)

            def three_pass(psum, parts, first=True, last=True):
                todo = [m for w_hi, w_lo, v_hi, v_lo in parts for m in ((w_lo, v_hi), (w_hi, v_hi), (w_hi, v_lo))]
                for i, (w, v) in enumerate(todo):
                    ins = nc.tensor.matmul(psum, w, v, start=first and i == 0, stop=last and i == len(todo) - 1)
                return ins

            def sum_squares(p):
                if not p.exists:
                    return
                pe.wait_ge(sq_ready, p.count(1, 1))
                if p.follows(1):
                    pe.wait_ge(ms_read, p.count(1, 0))
                tokens = xsq[:, p.slot % 2, :].rearrange("c (p j) -> c j p", j=TPP)
                for j in range(TPP):
                    last = nc.tensor.matmul(p_norm[:, j:j + 1], tokens[:, j, :], ones[:, 0:1],
                                            start=True, stop=True)
                last.then_inc(ms_ready, 1)

            def project_in(p, r, h):
                if not p.exists:
                    return
                pe.wait_ge(xn_hi_ready, p.count(1, 1))
                pe.wait_ge(xn_lo_ready, p.count(1, 1))
                if p.follows(1) or r or h:
                    pe.wait_ge(tanh_ready, p.count(4, 2 * r + h))
                v_hi = xn_hi[:, p.slot % 2, r * T:(r + 1) * T]
                v_lo = xn_lo[:, p.slot % 2, r * T:(r + 1) * T]
                cols = slice((HB + h) * 128, (HB + h + 1) * 128)
                three_pass(p_b[:, :], [(win_hi[:, cols], win_lo[:, cols], v_hi, v_lo)]
                           ).then_inc(b_ready, 1)
                if p.follows(1) or r or h:
                    pe.wait_ge(ab_ready, p.count(4, 2 * r + h))
                cols = slice(h * 128, (h + 1) * 128)
                three_pass(p_a[:, :], [(win_hi[:, cols], win_lo[:, cols], v_hi, v_lo)]
                           ).then_inc(a_ready, 1)

            def conv(p, r):
                if not p.exists:
                    return
                pairs = 2 if r == ROWS - 1 and p.next_exists() else 1
                pe.wait_ge(y_hi_ready, p.count(1, pairs))
                pe.wait_ge(y_lo_ready, p.count(1, pairs))
                if p.follows(2):
                    pe.wait_ge(z_ready[0], p.count(1, -1))
                cols = {tap: SHARED_COLS[r] if tap == SHARED else T for tap in PE_TAPS}
                taps = [(kh, kw) for kh, kw in PE_TAPS if r in p.tap_rows(kh) and cols[kh, kw]]
                for kh, kw in taps:
                    i = PE_TAPS.index((kh, kw))
                    at = ((p.slot % YRING) * ROWS + r + kh - 1) % (YRING * ROWS)
                    n = cols[kh, kw]
                    last = three_pass(p_conv[p.slot % 2][:, r, 0:n],
                                      [(diag_hi[:, i, :], diag_lo[:, i, :],
                                        y_hi[:, at, kw:kw + n], y_lo[:, at, kw:kw + n])],
                                      (kh, kw) == taps[0], (kh, kw) == taps[-1])
                last.then_inc(conv_ready, 1)

            def project_out(p, r):
                if not p.exists:
                    return
                for h in range(HB):
                    pe.wait_ge(z_ready[h], p.count(1, 1))
                if p.follows(1) or r:
                    pe.wait_ge(o_ready, p.count(2, r))
                cols = slice(r * T, (r + 1) * T)
                for h in range(HB):
                    last = nc.tensor.matmul(p_o[:, :], wout[:, h, :], z[:, h, p.slot % 2, cols],
                                            start=(h == 0), stop=(h == HB - 1))
                last.then_inc(p_o_ready, 1)

            def body(s):
                project_in(s.pair(2), 0, 0)
                project_out(s.pair(6), 0)
                project_in(s.pair(2), 0, 1)
                sum_squares(s.pair(0))
                conv(s.pair(4), 0)

                project_in(s.pair(2), 1, 0)
                project_out(s.pair(6), 1)
                project_in(s.pair(2), 1, 1)
                conv(s.pair(4), 1)

            run_steps(pe, B, PAIRS, body)


def kernel(x, L0_conv_g_norm, L0_conv_w_in, L0_conv_b_in, L0_conv_w_dw, L0_conv_b_dw, L0_conv_w_out, L0_conv_b_out):
    import numpy as np
    import concourse.bacc as bacc
    from concourse.bass_utils import run_bass_kernel_spmd

    x = np.ascontiguousarray(x)
    C = x.shape[1]
    H = L0_conv_w_dw.shape[0]
    HB = H // 128
    arrays = {
        "x": x,
        "g_norm": np.ascontiguousarray(L0_conv_g_norm).reshape(C, 1),
        "w_in_t": np.ascontiguousarray(np.asarray(L0_conv_w_in).T),
        "b_in": np.ascontiguousarray(np.asarray(L0_conv_b_in).reshape(2 * HB, 128).T),
        "w_dw": np.ascontiguousarray(np.asarray(L0_conv_w_dw).reshape(HB, 128, KH * KW).transpose(1, 0, 2)),
        "b_dw": np.ascontiguousarray(np.asarray(L0_conv_b_dw).reshape(HB, 128).T),
        "w_out_t": np.ascontiguousarray(np.asarray(L0_conv_w_out).T.reshape(HB, 128, C).transpose(1, 0, 2)),
        "b_out": np.ascontiguousarray(L0_conv_b_out).reshape(C, 1),
    }
    nc = bacc.Bacc("TRN2", target_bir_lowering=False, num_devices=1)
    args = [nc.dram_tensor(name, a.shape, mybir.dt.from_np(a.dtype), kind="ExternalInput").ap()
            for name, a in arrays.items()]
    out = nc.dram_tensor("out", x.shape, mybir.dt.float32, kind="ExternalOutput").ap()
    conv_block(nc, *args, out)
    r = run_bass_kernel_spmd(nc, [arrays], core_ids=[0])
    return r.results[0]["out"]
```
